# Optimizing a Trainium2 kernel written in Bass

```python
import numpy as np
import jax
import jax.numpy as jnp

def _softmax(x, axis=-1):
    return jax.nn.softmax(x, axis=axis)

def _gelu(x):
    return jax.nn.gelu(x, approximate=True)

def _silu(x):
    return jax.nn.silu(x)

def _sigmoid(x):
    return jax.nn.sigmoid(x)

def _layernorm(x, axis=-1, eps=1e-05):
    m = jnp.mean(x, axis=axis, keepdims=True)
    v = jnp.var(x, axis=axis, keepdims=True)
    return (x - m) / jnp.sqrt(v + eps)

def _scatter_add(tgt, idx, src, axis=0):
    return tgt.at[idx].add(src)

def _segment_sum(src, seg, n):
    return jax.ops.segment_sum(src, seg, n)
kernel_name = 'mk_dlrm_tower_d1_rec_r8_86a3d9'

def setup_inputs(seed: int=0):
    np.random.seed(seed)
    _w = jnp.asarray

    def _rec_inputs():
        import jax
        import jax.numpy as jnp
        _tk = jax.random.key(seed)
        dense_ctx = jax.random.normal(jax.random.fold_in(_tk, 190), (2048, 16), jnp.float32)
        ids = jnp.stack([jax.random.randint(jax.random.fold_in(_tk, 200 + f), (2048,), 0, v, jnp.int32) for f, v in enumerate([1000, 125000, 1000, 1250, 12500, 1250, 12500, 1250, 1250, 1250, 12500, 1000, 1000, 1000, 1250, 12500, 1250, 1000, 12500, 1000, 1000, 12500, 1250, 1250, 1000, 1000, 1000])], axis=1)
        tbl_0 = 0.05 * jax.random.normal(jax.random.fold_in(_tk, 500 + 0), (1000, 128), jnp.float32)
        tbl_1 = 0.05 * jax.random.normal(jax.random.fold_in(_tk, 500 + 1), (125000, 128), jnp.float32)
        tbl_2 = 0.05 * jax.random.normal(jax.random.fold_in(_tk, 500 + 2), (1000, 128), jnp.float32)
        tbl_3 = 0.05 * jax.random.normal(jax.random.fold_in(_tk, 500 + 3), (1250, 128), jnp.float32)
        tbl_4 = 0.05 * jax.random.normal(jax.random.fold_in(_tk, 500 + 4), (12500, 128), jnp.float32)
        tbl_5 = 0.05 * jax.random.normal(jax.random.fold_in(_tk, 500 + 5), (1250, 128), jnp.float32)
        tbl_6 = 0.05 * jax.random.normal(jax.random.fold_in(_tk, 500 + 6), (12500, 128), jnp.float32)
        tbl_7 = 0.05 * jax.random.normal(jax.random.fold_in(_tk, 500 + 7), (1250, 128), jnp.float32)
        tbl_8 = 0.05 * jax.random.normal(jax.random.fold_in(_tk, 500 + 8), (1250, 128), jnp.float32)
        tbl_9 = 0.05 * jax.random.normal(jax.random.fold_in(_tk, 500 + 9), (1250, 128), jnp.float32)
        tbl_10 = 0.05 * jax.random.normal(jax.random.fold_in(_tk, 500 + 10), (12500, 128), jnp.float32)
        tbl_11 = 0.05 * jax.random.normal(jax.random.fold_in(_tk, 500 + 11), (1000, 128), jnp.float32)
        tbl_12 = 0.05 * jax.random.normal(jax.random.fold_in(_tk, 500 + 12), (1000, 128), jnp.float32)
        tbl_13 = 0.05 * jax.random.normal(jax.random.fold_in(_tk, 500 + 13), (1000, 128), jnp.float32)
        tbl_14 = 0.05 * jax.random.normal(jax.random.fold_in(_tk, 500 + 14), (1250, 128), jnp.float32)
        tbl_15 = 0.05 * jax.random.normal(jax.random.fold_in(_tk, 500 + 15), (12500, 128), jnp.float32)
        tbl_16 = 0.05 * jax.random.normal(jax.random.fold_in(_tk, 500 + 16), (1250, 128), jnp.float32)
        tbl_17 = 0.05 * jax.random.normal(jax.random.fold_in(_tk, 500 + 17), (1000, 128), jnp.float32)
        tbl_18 = 0.05 * jax.random.normal(jax.random.fold_in(_tk, 500 + 18), (12500, 128), jnp.float32)
        tbl_19 = 0.05 * jax.random.normal(jax.random.fold_in(_tk, 500 + 19), (1000, 128), jnp.float32)
        tbl_20 = 0.05 * jax.random.normal(jax.random.fold_in(_tk, 500 + 20), (1000, 128), jnp.float32)
        tbl_21 = 0.05 * jax.random.normal(jax.random.fold_in(_tk, 500 + 21), (12500, 128), jnp.float32)
        tbl_22 = 0.05 * jax.random.normal(jax.random.fold_in(_tk, 500 + 22), (1250, 128), jnp.float32)
        tbl_23 = 0.05 * jax.random.normal(jax.random.fold_in(_tk, 500 + 23), (1250, 128), jnp.float32)
        tbl_24 = 0.05 * jax.random.normal(jax.random.fold_in(_tk, 500 + 24), (1000, 128), jnp.float32)
        tbl_25 = 0.05 * jax.random.normal(jax.random.fold_in(_tk, 500 + 25), (1000, 128), jnp.float32)
        tbl_26 = 0.05 * jax.random.normal(jax.random.fold_in(_tk, 500 + 26), (1000, 128), jnp.float32)
        _rk = jax.random.fold_in(_tk, 7)
        W_top1 = 0.0161733 * jax.random.normal(jax.random.fold_in(_tk, 801), (3823, 512), jnp.float32)
        W_top2 = 0.0441942 * jax.random.normal(jax.random.fold_in(_tk, 802), (512, 256), jnp.float32)
        W_top3 = 0.0625 * jax.random.normal(jax.random.fold_in(_tk, 803), (256, 1), jnp.float32)
        b_top1 = jnp.zeros((512,), jnp.float32)
        b_top2 = jnp.zeros((256,), jnp.float32)
        return (dense_ctx, ids, tbl_0, tbl_1, tbl_2, tbl_3, tbl_4, tbl_5, tbl_6, tbl_7, tbl_8, tbl_9, tbl_10, tbl_11, tbl_12, tbl_13, tbl_14, tbl_15, tbl_16, tbl_17, tbl_18, tbl_19, tbl_20, tbl_21, tbl_22, tbl_23, tbl_24, tbl_25, tbl_26, W_top1, b_top1, W_top2, b_top2, W_top3)
    dense_ctx, ids, tbl_0, tbl_1, tbl_2, tbl_3, tbl_4, tbl_5, tbl_6, tbl_7, tbl_8, tbl_9, tbl_10, tbl_11, tbl_12, tbl_13, tbl_14, tbl_15, tbl_16, tbl_17, tbl_18, tbl_19, tbl_20, tbl_21, tbl_22, tbl_23, tbl_24, tbl_25, tbl_26, W_top1, b_top1, W_top2, b_top2, W_top3 = _rec_inputs()

    def _L0_rec_setup():
        import jax, jax.numpy as jnp
        import numpy as np
        NUM_FEATURES = 27
        FEATURE_DIM = 128
        BATCH = 2048
        _TRIU_I, _TRIU_J = np.triu_indices(NUM_FEATURES, k=1)
        key = jax.random.key(seed)
        embeddings = jax.random.normal(key, (BATCH, NUM_FEATURES, FEATURE_DIM), dtype=jnp.float32)
        return {'embeddings': embeddings}
    _L0_rec_all = _L0_rec_setup()
    _L0_rec_in = {k: v for k, v in _L0_rec_all.items() if k in ()}
    del _L0_rec_all
    return {'dense_ctx': dense_ctx, 'ids': ids, 'tbl_0': tbl_0, 'tbl_1': tbl_1, 'tbl_2': tbl_2, 'tbl_3': tbl_3, 'tbl_4': tbl_4, 'tbl_5': tbl_5, 'tbl_6': tbl_6, 'tbl_7': tbl_7, 'tbl_8': tbl_8, 'tbl_9': tbl_9, 'tbl_10': tbl_10, 'tbl_11': tbl_11, 'tbl_12': tbl_12, 'tbl_13': tbl_13, 'tbl_14': tbl_14, 'tbl_15': tbl_15, 'tbl_16': tbl_16, 'tbl_17': tbl_17, 'tbl_18': tbl_18, 'tbl_19': tbl_19, 'tbl_20': tbl_20, 'tbl_21': tbl_21, 'tbl_22': tbl_22, 'tbl_23': tbl_23, 'tbl_24': tbl_24, 'tbl_25': tbl_25, 'tbl_26': tbl_26, 'W_top1': W_top1, 'b_top1': b_top1, 'W_top2': W_top2, 'b_top2': b_top2, 'W_top3': W_top3}

def reference(dense_ctx, ids, tbl_0, tbl_1, tbl_2, tbl_3, tbl_4, tbl_5, tbl_6, tbl_7, tbl_8, tbl_9, tbl_10, tbl_11, tbl_12, tbl_13, tbl_14, tbl_15, tbl_16, tbl_17, tbl_18, tbl_19, tbl_20, tbl_21, tbl_22, tbl_23, tbl_24, tbl_25, tbl_26, W_top1, b_top1, W_top2, b_top2, W_top3):
    import jax
    import jax.numpy as jnp

    def _L0_rec_ref(embeddings):
        import jax, jax.numpy as jnp
        import numpy as np
        NUM_FEATURES = 27
        FEATURE_DIM = 128
        BATCH = 2048
        _TRIU_I, _TRIU_J = np.triu_indices(NUM_FEATURES, k=1)
        B = embeddings.shape[0]
        interactions = jnp.einsum('bfd,bgd->bfg', embeddings, embeddings)
        flat_interactions = interactions[:, _TRIU_I, _TRIU_J]
        flat_embeddings = embeddings.reshape(B, -1)
        return jnp.concatenate([flat_embeddings, flat_interactions], axis=1)
    e = jnp.stack([tbl_0[ids[:, 0]], tbl_1[ids[:, 1]], tbl_2[ids[:, 2]], tbl_3[ids[:, 3]], tbl_4[ids[:, 4]], tbl_5[ids[:, 5]], tbl_6[ids[:, 6]], tbl_7[ids[:, 7]], tbl_8[ids[:, 8]], tbl_9[ids[:, 9]], tbl_10[ids[:, 10]], tbl_11[ids[:, 11]], tbl_12[ids[:, 12]], tbl_13[ids[:, 13]], tbl_14[ids[:, 14]], tbl_15[ids[:, 15]], tbl_16[ids[:, 16]], tbl_17[ids[:, 17]], tbl_18[ids[:, 18]], tbl_19[ids[:, 19]], tbl_20[ids[:, 20]], tbl_21[ids[:, 21]], tbl_22[ids[:, 22]], tbl_23[ids[:, 23]], tbl_24[ids[:, 24]], tbl_25[ids[:, 25]], tbl_26[ids[:, 26]]], axis=1)
    z = _L0_rec_ref(e)
    z = z.reshape(z.shape[0], -1)
    h = jnp.concatenate([z, dense_ctx], axis=1)
    h = jnp.maximum(h @ W_top1 + b_top1, 0.0)
    h = jnp.maximum(h @ W_top2 + b_top2, 0.0)
    y = h @ W_top3
    return y

_drawn_inputs = setup_inputs


def setup_inputs(seed=0):
    import zlib

    import numpy as np

    out = dict(_drawn_inputs(seed))
    spreads = {'b_top1': (0.0, 0.1), 'b_top2': (0.0, 0.1)}
    factors = {}
    for name, (base, spread) in spreads.items():
        noise = np.random.default_rng([zlib.crc32(name.encode()), seed]).standard_normal(out[name].shape)
        drawn = base * np.exp(spread * noise) if base else spread * noise
        out[name] = jnp.asarray(drawn.astype(out[name].dtype))
    for name, factor in factors.items():
        out[name] = (out[name] * factor).astype(out[name].dtype)
    return out
```

```python
from contextlib import ExitStack

import numpy as np

import concourse.bass as bass
from concourse import mybir

F32 = mybir.dt.float32
F32R = mybir.dt.float32r
ALU = mybir.AluOpType
ACT = mybir.ActivationFunctionType

P = 128
NF = 27
BATCH, DENSE, H1, H2 = 2048, 16, 512, 256
NC = BATCH // P
NPAIR = NF * (NF - 1) // 2
SHIFTS = NPAIR // NF
TAIL = NPAIR + DENSE + 1
KT = -(-TAIL // P)
KLAST = TAIL - (KT - 1) * P
NK = NF + KT
GROUP = 4
NG = -(-NF // GROUP)
FP = 32
Q = P // FP
QUADS = P // (Q * Q)
SLOTS = 18
STAGE = 4


def features(g):
    return range(g * GROUP, min((g + 1) * GROUP, NF))


def mlp_tower(nc, t, out):
    ids = t["ids"].rearrange("(c p) f -> c p f", p=P)
    dense = t["dense_ctx"].rearrange("(c t j) d -> c j t d", t=FP, j=Q)

    with ExitStack() as ctx:
        def sb(name, shape, dt=F32):
            return ctx.enter_context(nc.sbuf_tensor(name, shape, dt))

        def psum(name, shape):
            return ctx.enter_context(nc.psum_tensor(name, shape, F32))

        def sem(name):
            return ctx.enter_context(nc.semaphore(name))

        w1h = sb("w1_high", [P, NK, H1], F32R)
        w1l = sb("w1_low", [P, NK, H1], F32R)
        xs = [sb(f"x_split{i}", [P, 2, P, FP], F32R) for i in range(2)]
        rows = sb("rows", [P, SLOTS, P])
        AW = (NF + SHIFTS) * NF
        arena = sb("arena", [P, AW + 2 * H1])
        w_stage = arena[:, 0:STAGE * H1].rearrange("p (s n) -> p s n", s=STAGE)
        d_feat = arena[:, 0:NF * FP].rearrange("p (g t) -> p g t", t=FP)
        full = arena[:, 0:AW].rearrange("p (g f) -> p g f", f=NF)
        d_samp = arena[:, AW:AW + NF * FP].rearrange("p (g f) -> p g f", f=FP)
        h1 = arena[:, AW:AW + H1]
        h1t = arena[:, AW + H1:AW + 2 * H1].rearrange("p (k b) -> p k b", b=P)
        h2 = arena[:, AW:AW + H2]
        packed = sb("packed", [P, KT * P])
        zh = sb("pairs_high", [P, KT, P], F32R)
        zl = sb("pairs_low", [P, KT, P], F32R)
        w2 = sb("w2", [P, H1 // P, H2])
        b2 = sb("b2", [P, H2])
        w3 = sb("w3", [P, H2])
        ident = sb("ident", [P, P])
        idx = [sb(f"idx{i}", [P, NF], t["ids"].dtype) for i in range(2)]
        y = sb("y", [P, NC])
        yt = sb("y_turned", [NC, P])

        acc = [psum(f"acc{i}", [P, H1]) for i in range(2)]
        xt = psum("x_turned_bank", [P, GROUP, P])
        gram = [psum(f"gram{i}", [P, Q, 2, P]) for i in range(2)]
        misc = psum("misc", [P, H1])
        misc_turn = misc[:, :].rearrange("p (k b) -> p k b", b=P)

        gathered = [sem(f"gathered{s}") for s in range(SLOTS)]
        idx_in = [sem(f"idx_in{i}") for i in range(2)]
        w_in = [sem(f"w_in{s}") for s in range(STAGE)]
        w_high, w_low = sem("w_high"), sem("w_low")
        consts_in, cleared = sem("consts_in"), sem("cleared")
        dense_in, slots_freed = sem("dense_in"), sem("slots_freed")
        x_turned, x_high, x_low = sem("x_turned"), sem("x_high"), sem("x_low")
        gram_done, gram_read = sem("gram_done"), sem("gram_read")
        gram_half = sem("gram_half")
        d_turned, full_done, pack_done = sem("d_turned"), sem("full_done"), sem("pack_done")
        pair_turned, pair_high, pair_low = sem("pair_turned"), sem("pair_high"), sem("pair_low")
        acc_done, h1_done = sem("acc_done"), sem("h1_done")
        h1_turned, h1t_done = sem("h1_turned"), sem("h1t_done")
        fc2_done, h2_done, y_done = sem("fc2_done"), sem("h2_done"), sem("y_done")
        y_turned, y_copied, stored = sem("y_turned"), sem("y_copied"), sem("stored")

        CONSTS = 4 * 16

        def slot_of(par, f):
            n = par * NF + f
            return n % SLOTS, n // SLOTS

        USES = 2 * NF // SLOTS


        block = ctx.enter_context(nc.Block())

        @block.sync
        def _(sp):
            def load_ids(m, par, c):
                sp.dma_start(idx[par][:, :], ids[c]).then_inc(idx_in[par], 16)

            def load_dense(c):
                for j in range(Q):
                    sp.dma_start(packed[FP * j:FP * j + FP, NPAIR:NPAIR + DENSE],
                                 dense[c, j]).then_inc(dense_in, 16)

            load_ids(0, 0, 0)
            load_ids(0, 1, 1)
            sp.dma_start(ident[:, :], t["ident"]).then_inc(consts_in, 16)
            for k in range(NK):
                if k >= STAGE:
                    sp.wait_ge(w_low, k - STAGE + 1)
                if k < NF:
                    sp.dma_start(w_stage[:, k % STAGE], t["w1"][k * P:(k + 1) * P]).then_inc(w_in[k % STAGE], 16)
                else:
                    n = P if k < NK - 1 else KLAST
                    a = (k - NF) * P
                    sp.dma_start(w_stage[0:n, k % STAGE], t["w1_tail"][a:a + n]).then_inc(w_in[k % STAGE], 16)
                if k == GROUP:
                    sp.dma_start(w2[:, :, :], t["W_top2"].rearrange("(k p) n -> p k n", p=P)).then_inc(consts_in, 16)
                    sp.dma_start(b2[:, :], t["b_top2"].to_broadcast([P, H2])).then_inc(consts_in, 16)
                    sp.dma_start(w3[:, :], t["W_top3"].to_broadcast([P, H2])).then_inc(consts_in, 16)
            sp.wait_ge(cleared, 1)
            load_dense(0)

            def chunk(m, par, last=False):
                c = 2 * m + par
                if not last:
                    sp.wait_ge(x_turned, (c + 1) * NF)
                    load_ids(m, par, c + 2)
                if not (last and par == 1):
                    sp.wait_ge(pair_turned, c + 1)
                    load_dense(c + 1)

            with sp.Fori(0, NC // 2 - 1) as m:
                for par in range(2):
                    chunk(m, par)
            for par in range(2):
                chunk(NC // 2 - 1, par, last=True)
            sp.wait_ge(y_copied, 1)
            sp.dma_start(out.rearrange("(c p) o -> c (p o)", p=P), yt[:, :]).then_inc(stored, 16)
            sp.wait_ge(stored, 16)

        @block.gpsimd
        def _(pool):
            def gathers(m, par, first=False):
                pool.wait_ge(idx_in[par], 16 * (m + 1))
                for f in range(NF):
                    slot, _ = slot_of(par, f)
                    n = par * NF + f - SLOTS
                    if n >= 0 or not first:
                        pool.wait_ge(x_turned, m * (2 * NF) + n + 1)
                    if not first:
                        pool.sem_inc(slots_freed, 1)
                    nc.gpsimd.indirect_dma_start(
                        rows[:, slot, :], None, t[f"tbl_{f}"],
                        bass.IndirectOffsetOnAxis(ap=idx[par][:, f:f + 1], axis=0),
                    ).then_inc(gathered[slot], 16)

            for par in range(2):
                gathers(0, par, first=True)
            with pool.Fori(1, NC // 2) as m:
                for par in range(2):
                    gathers(m, par)

        @block.tensor
        def _(pe):
            def turn(m, par, g):
                for f in features(g):
                    slot, use = slot_of(par, f)
                    pe.wait_ge(gathered[slot], (m * USES + use + 1) * 16)
                    if f == g * GROUP and not (isinstance(m, int) and m == 0 and par == 0 and g == 0):
                        pe.wait_ge(x_low, (m * 2 + par) * NG + g)
                    nc.tensor.transpose(xt[:, f % GROUP, :], rows[:, slot, :], ident[:, :]).then_inc(x_turned, 1)

            def fc1(m, par, g, part, first=False):
                for f in list(features(g))[2 * part:2 * part + 2]:
                    if f == 0:
                        if not first:
                            pe.wait_ge(h1_done, m * 2 + par - 1)
                    if f % GROUP == 0:
                        pe.wait_ge(x_low, (m * 2 + par) * NG + g + 1)
                    if first and par == 0:
                        pe.wait_ge(w_low, f + 1)
                    xh, xl = xs[par][:, 0, :, f], xs[par][:, 1, :, f]
                    nc.tensor.matmul(acc[par][:, :], xh, w1h[:, f, :], start=f == 0, stop=False)
                    nc.tensor.matmul(acc[par][:, :], xh, w1l[:, f, :], start=False, stop=False)
                    nc.tensor.matmul(acc[par][:, :], xl, w1h[:, f, :], start=False, stop=False)

            def grams(m, par, q):
                if not (isinstance(m, int) and m == 0 and par == 0 and q < 2):
                    pe.wait_ge(gram_read, (m * 2 + par) * QUADS + q - 1)
                for i in range(Q):
                    s = (q * Q + i) * Q
                    mm = nc.tensor.matmul(gram[q % 2][:, i, :, :], xs[par][:, 0, s:s + Q, :],
                                          xs[par][:, :, s:s + Q, :], start=True, stop=True)
                mm.then_inc(gram_done, 1)

            def turn_pairs(m, par, c):
                pe.wait_ge(pack_done, c + 1)
                pe.wait_ge(dense_in, (c + 1) * (Q * 16))
                if not (isinstance(c, int) and c == 0):
                    pe.wait_ge(h2_done, c)
                for k in range(KT):
                    tr = nc.tensor.transpose(misc_turn[:, k, :], packed[:, k * P:(k + 1) * P], ident[:, :])
                tr.then_inc(pair_turned, 1)

            def fc1_pairs(m, par, c):
                pe.wait_ge(pair_low, c + 1)
                if isinstance(c, int) and c == 0:
                    pe.wait_ge(w_low, NK)
                for k in range(KT):
                    n = P if k < KT - 1 else KLAST
                    nc.tensor.matmul(acc[par][:, :], zh[0:n, k, :], w1h[0:n, NF + k, :], start=False, stop=False)
                    nc.tensor.matmul(acc[par][:, :], zh[0:n, k, :], w1l[0:n, NF + k, :], start=False, stop=False)
                    mm = nc.tensor.matmul(acc[par][:, :], zl[0:n, k, :], w1h[0:n, NF + k, :],
                                          start=False, stop=k == KT - 1)
                mm.then_inc(acc_done, 1)

            def turn_h1(c):
                pe.wait_ge(h1_done, c + 1)
                for k in range(H1 // P):
                    tr = nc.tensor.transpose(misc_turn[:, k, :], h1[:, k * P:(k + 1) * P], ident[:, :])
                tr.then_inc(h1_turned, 1)

            def fc2(c):
                pe.wait_ge(h1t_done, c + 1)
                if isinstance(c, int) and c == 0:
                    pe.wait_ge(consts_in, CONSTS)
                for k in range(H1 // P):
                    mm = nc.tensor.matmul(misc[:, 0:H2], h1t[:, k, :], w2[:, k, :], start=k == 0, stop=k == H1 // P - 1)
                mm.then_inc(fc2_done, 1)

            def before(m, par):
                return (m, 0) if par else (m - 1, 1)

            def chunk(m, par, first=False, last=False):
                c = 2 * m + par
                prev = not (first and par == 0)
                prev2 = not first
                pm, pp = before(m, par)
                for g in range(NG):
                    if g + 1 < NG:
                        turn(m, par, g + 1)
                    elif not (last and par == 1):
                        turn(*((m, 1) if par == 0 else (m + 1, 0)), 0)
                    if g == 0 and prev2:
                        turn_h1(c - 2)
                    if prev and g < QUADS // 2:
                        grams(pm, pp, 2 * g)
                    if g == 5 and prev:
                        turn_pairs(pm, pp, c - 1)
                    if g == 6 and prev:
                        fc1_pairs(pm, pp, c - 1)
                    fc1(m, par, g, 0, first)
                    if prev and g < QUADS // 2:
                        grams(pm, pp, 2 * g + 1)
                    if g == 1 and prev2:
                        fc2(c - 2)
                    fc1(m, par, g, 1, first)

            pe.wait_ge(consts_in, 16)
            turn(0, 0, 0)
            pe.wait_ge(cleared, 1)
            for par in range(2):
                chunk(0, par, first=True)
            with pe.Fori(1, NC // 2 - 1) as m:
                for par in range(2):
                    chunk(m, par)
            for par in range(2):
                chunk(NC // 2 - 1, par, last=True)
            turn_h1(NC - 2)
            for q in range(QUADS):
                grams(NC // 2 - 1, 1, q)
                if q == 2:
                    fc2(NC - 2)
            turn_pairs(NC // 2 - 1, 1, NC - 1)
            fc1_pairs(NC // 2 - 1, 1, NC - 1)
            turn_h1(NC - 1)
            fc2(NC - 1)
            pe.wait_ge(y_done, NC)
            nc.tensor.transpose(misc[0:NC, 0:P], y[:, :], ident[:, :]).then_inc(y_turned, 1)

        @block.scalar
        def _(act):
            def high(m, par, g):
                n = len(features(g))
                a = g * GROUP
                act.wait_ge(x_turned, (m * 2 + par) * NF + a + n)
                nc.scalar.copy(xs[par][:, 0, :, a:a + n].rearrange("p s f -> p f s"), xt[:, 0:n, :]).then_inc(x_high, 1)

            def w_split(k):
                n = P if k < NK - 1 else KLAST
                act.wait_ge(w_in[k % STAGE], 16 * (k // STAGE + 1))
                nc.scalar.copy(w1h[0:n, k, :], w_stage[0:n, k % STAGE, :]).then_inc(w_high, 1)

            def half_high(c, q):
                act.wait_ge(gram_done, c * QUADS + q + 1)
                if q == 0:
                    if isinstance(c, int) and c == 0:
                        act.wait_ge(w_low, NK)
                    else:
                        act.wait_ge(pack_done, c)
                for j in range(Q):
                    a = FP * j
                    d = d_feat[a:a + FP, :, q * Q:(q + 1) * Q].rearrange("p g t -> p t g")
                    ins = nc.scalar.mul(d, gram[q % 2][a:a + FP, :, 0, a:a + NF], 0.5)
                ins.then_inc(gram_half, 1)

            def pack(c):
                act.wait_ge(full_done, 2 * (c + 1))
                if not (isinstance(c, int) and c == 0):
                    act.wait_ge(pair_turned, c)
                diagonals = bass.AP(full.tensor, full.offset + NF, [list(full.ap[0]), [NF, SHIFTS], [NF + 1, NF]])
                nc.scalar.copy(packed[:, 0:NPAIR].rearrange("p (k f) -> p k f", f=NF), diagonals).then_inc(pack_done, 1)

            def pairs_high(c):
                act.wait_ge(pair_turned, c + 1)
                nc.scalar.copy(zh[:, :, :].rearrange("p k (t j) -> p k j t", j=Q),
                               misc_turn[:, 0:KT, :].rearrange("p k (j t) -> p k j t", j=Q)).then_inc(pair_high, 1)

            def relu1(par, c):
                act.wait_ge(acc_done, c + 1)
                nc.scalar.activation(h1, acc[par][:, :], ACT.Relu).then_inc(h1_done, 1)

            def h1_copy(c):
                act.wait_ge(h1_turned, c + 1)
                nc.scalar.copy(h1t, misc_turn[:, :, :]).then_inc(h1t_done, 1)

            def chunk(m, par, first=False, last=False):
                c = 2 * m + par
                prev = not (first and par == 0)
                prev2 = not first
                for g in range(NG):
                    if not prev:
                        for k in range((g + 1) * GROUP, min((g + 2) * GROUP, NK)):
                            w_split(k)
                    if g + 1 < NG:
                        high(m, par, g + 1)
                    elif not (last and par == 1):
                        high(*((m, 1) if par == 0 else (m + 1, 0)), 0)
                    if g == 0 and prev2:
                        h1_copy(c - 2)
                    if prev and g < QUADS // 2:
                        half_high(c - 1, 2 * g)
                        half_high(c - 1, 2 * g + 1)
                    if g == 4 and prev:
                        pack(c - 1)
                    if g == 5 and prev:
                        pairs_high(c - 1)
                    if g == 6 and prev:
                        relu1(1 - par, c - 1)

            for k in range(GROUP):
                w_split(k)
            high(0, 0, 0)
            for par in range(2):
                chunk(0, par, first=True)
            with act.Fori(1, NC // 2 - 1) as m:
                for par in range(2):
                    chunk(m, par)
            for par in range(2):
                chunk(NC // 2 - 1, par, last=True)
            h1_copy(NC - 2)
            for q in range(QUADS):
                half_high(NC - 1, q)
            pack(NC - 1)
            pairs_high(NC - 1)
            relu1(1, NC - 1)
            h1_copy(NC - 1)

        @block.vector
        def _(dve):
            def low(m, par, g):
                n = len(features(g))
                a = g * GROUP
                dve.wait_ge(x_high, (m * 2 + par) * NG + g + 1)
                nc.vector.tensor_tensor(xs[par][:, 1, :, a:a + n].rearrange("p s f -> p f s"), xt[:, 0:n, :],
                                        xs[par][:, 0, :, a:a + n].rearrange("p s f -> p f s").bitcast(F32),
                                        ALU.subtract).then_inc(x_low, 1)

            def w_split(k):
                n = P if k < NK - 1 else KLAST
                dve.wait_ge(w_high, k + 1)
                nc.vector.tensor_tensor(w1l[0:n, k, :], w_stage[0:n, k % STAGE, :], w1h[0:n, k, :].bitcast(F32),
                                        ALU.subtract).then_inc(w_low, 1)

            def add_low(c, q):
                dve.wait_ge(gram_half, c * QUADS + q + 1)
                for j in range(Q):
                    a = FP * j
                    d = d_feat[a:a + FP, :, q * Q:(q + 1) * Q].rearrange("p g t -> p t g")
                    ins = nc.vector.tensor_tensor(d, gram[q % 2][a:a + FP, :, 1, a:a + NF], d, ALU.add)
                ins.then_inc(gram_read, 1)

            def fill_full(c):
                dve.wait_ge(gram_read, (c + 1) * QUADS)
                if not (isinstance(c, int) and c == 0):
                    dve.wait_ge(h2_done, c)
                    dve.wait_ge(y_done, c)
                nc.vector.transpose(d_samp.rearrange("p g f -> p (g f)"), d_feat.rearrange("p g t -> p (g t)")).then_inc(d_turned, 1)
                dve.wait_ge(d_turned, c + 1)
                for a, n in ((0, NF), (NF, SHIFTS)):
                    nc.vector.tensor_tensor(full[:, a:a + n, :], d_samp[:, 0:n, 0:NF],
                                            d_samp[:, 0:NF, 0:n].rearrange("p f g -> p g f"),
                                            ALU.add).then_inc(full_done, 1)

            def pairs_low(c):
                dve.wait_ge(pair_high, c + 1)
                nc.vector.tensor_tensor(zl[:, :, :].rearrange("p k (t j) -> p k j t", j=Q),
                                        misc_turn[:, 0:KT, :].rearrange("p k (j t) -> p k j t", j=Q),
                                        zh[:, :, :].rearrange("p k (t j) -> p k j t", j=Q).bitcast(F32),
                                        ALU.subtract).then_inc(pair_low, 1)

            def result(c):
                dve.wait_ge(fc2_done, c + 1)
                if isinstance(c, int) and c == 0:
                    dve.wait_ge(consts_in, CONSTS)
                nc.vector.tensor_tensor(h2, misc[:, 0:H2], b2[:, :], ALU.add).then_inc(h2_done, 1)
                dve.wait_ge(h2_done, c + 1)
                col = y[:, c:c + 1] if isinstance(c, int) else y[:, bass.ds(c, 1)]
                nc.vector.scalar_tensor_tensor(h2, h2, 0.0, w3[:, :], ALU.max, ALU.mult, accum_out=col).then_inc(y_done, 1)

            def chunk(m, par, first=False, last=False):
                c = 2 * m + par
                prev = not (first and par == 0)
                prev2 = not first
                for g in range(NG):
                    if not prev:
                        for k in range((g + 1) * GROUP, min((g + 2) * GROUP, NK)):
                            w_split(k)
                    if g + 1 < NG:
                        low(m, par, g + 1)
                    elif not (last and par == 1):
                        low(*((m, 1) if par == 0 else (m + 1, 0)), 0)
                    if prev and g < QUADS // 2:
                        add_low(c - 1, 2 * g)
                        add_low(c - 1, 2 * g + 1)
                    if g == 1 and prev2:
                        result(c - 2)
                    if g == 3 and prev:
                        fill_full(c - 1)
                    if g == 5 and prev:
                        pairs_low(c - 1)

            for x in xs:
                for part in range(2):
                    nc.vector.memset(x[:, part, :, NF:FP].bitcast(F32), 0.0)
            for k in range(GROUP):
                w_split(k)
            nc.vector.memset(packed[:, NPAIR + DENSE:TAIL], 1.0)
            nc.vector.memset(packed[:, TAIL:], 0.0).then_inc(cleared, 1)
            low(0, 0, 0)
            for par in range(2):
                chunk(0, par, first=True)
            with dve.Fori(1, NC // 2 - 1) as m:
                for par in range(2):
                    chunk(m, par)
            for par in range(2):
                chunk(NC // 2 - 1, par, last=True)
            for q in range(4):
                add_low(NC - 1, q)
            result(NC - 2)
            for q in range(4, QUADS):
                add_low(NC - 1, q)
            fill_full(NC - 1)
            pairs_low(NC - 1)
            result(NC - 1)
            dve.wait_ge(y_turned, 1)
            nc.vector.tensor_copy(yt[:, :], misc[0:NC, 0:P]).then_inc(y_copied, 1)


def kernel(**inputs):
    import numpy as _np
    import concourse.bacc as _bacc
    from concourse import mybir as _mybir
    from concourse.bass_utils import run_bass_kernel_spmd as _run

    nc = _bacc.Bacc("TRN2", target_bir_lowering=False, num_devices=1, dynamic_dma_scratch_size=8192)
    given = {k: _np.ascontiguousarray(v) for k, v in inputs.items()}
    w1 = given.pop("W_top1")
    b1 = given.pop("b_top1")
    at = {}
    for i, j in zip(*_np.triu_indices(NF, k=1)):
        at[int(i), int(j)] = len(at)
    order = [at[min(f, (f + k) % NF), max(f, (f + k) % NF)] for k in range(1, SHIFTS + 1) for f in range(NF)]
    pair_rows = w1[NF * P:NF * P + NPAIR][_np.array(order)]
    given["w1"] = w1[:NF * P]
    given["w1_tail"] = _np.concatenate([pair_rows, w1[NF * P + NPAIR:], b1[None, :]], axis=0)
    given["b_top2"] = given["b_top2"].reshape(1, H2)
    given["W_top3"] = given["W_top3"].reshape(1, H2)
    given["ident"] = _np.eye(P, dtype=_np.float32)
    arrays, tensors = {}, {}
    for name, a in given.items():
        a = _np.ascontiguousarray(a)
        arrays[f"in_{name}_dram"] = a
        tensors[name] = nc.dram_tensor(f"in_{name}_dram", a.shape, _mybir.dt.from_np(a.dtype), kind="ExternalInput").ap()
    out = nc.dram_tensor("out_0_dram", (BATCH, 1), F32, kind="ExternalOutput").ap()
    mlp_tower(nc, tensors, out)
    r = _run(nc, [arrays], core_ids=[0])
    return r.results[0]["out_0_dram"]
```

```python
from contextlib import ExitStack

import numpy as np

import concourse.bass as bass
from concourse import mybir

F32 = mybir.dt.float32
F32R = mybir.dt.float32r
ALU = mybir.AluOpType
ACT = mybir.ActivationFunctionType

P = 128
NF = 27
BATCH, DENSE, H1, H2 = 2048, 16, 512, 256
NC = BATCH // P
NPAIR = NF * (NF - 1) // 2
SHIFTS = NPAIR // NF
TAIL = NPAIR + DENSE + 1
KT = -(-TAIL // P)
KLAST = TAIL - (KT - 1) * P
NK = NF + KT
GROUP = 4
NG = -(-NF // GROUP)
FP = 32
Q = P // FP
QUADS = P // (Q * Q)
SLOTS = 18
AHEAD = 6
STAGE = 4


def features(g):
    return range(g * GROUP, min((g + 1) * GROUP, NF))


def mlp_tower(nc, t, out):
    ids = t["ids"].rearrange("(c p) f -> c p f", p=P)
    dense = t["dense_ctx"].rearrange("(c t j) d -> c j t d", t=FP, j=Q)

    with ExitStack() as ctx:
        def sb(name, shape, dt=F32):
            return ctx.enter_context(nc.sbuf_tensor(name, shape, dt))

        def psum(name, shape):
            return ctx.enter_context(nc.psum_tensor(name, shape, F32))

        def sem(name):
            return ctx.enter_context(nc.semaphore(name))

        w1h = sb("w1_high", [P, NK, H1], F32R)
        w1l = sb("w1_low", [P, NK, H1], F32R)
        xs = [sb(f"x_split{i}", [P, 2, P, FP], F32R) for i in range(2)]
        rows = sb("rows", [P, SLOTS, P])
        AW = (NF + SHIFTS) * NF
        arena = sb("arena", [P, AW + 2 * H1])
        w_stage = arena[:, 0:STAGE * H1].rearrange("p (s n) -> p s n", s=STAGE)
        d_feat = arena[:, 0:NF * FP].rearrange("p (g t) -> p g t", t=FP)
        full = arena[:, 0:AW].rearrange("p (g f) -> p g f", f=NF)
        d_samp = arena[:, AW:AW + NF * FP].rearrange("p (g f) -> p g f", f=FP)
        h1 = arena[:, AW:AW + H1]
        h1t = arena[:, AW + H1:AW + 2 * H1].rearrange("p (k b) -> p k b", b=P)
        h2 = arena[:, AW:AW + H2]
        packed = sb("packed", [P, KT * P])
        zh = sb("pairs_high", [P, KT, P], F32R)
        zl = sb("pairs_low", [P, KT, P], F32R)
        w2 = sb("w2", [P, H1 // P, H2])
        b2 = sb("b2", [P, H2])
        w3 = sb("w3", [P, H2])
        ident = sb("ident", [P, P])
        idx = [sb(f"idx{i}", [P, NF], t["ids"].dtype) for i in range(2)]
        y = sb("y", [P, NC])
        yt = sb("y_turned", [NC, P])

        acc = [psum(f"acc{i}", [P, H1]) for i in range(2)]
        xt = psum("x_turned_bank", [P, GROUP, P])
        gram = [psum(f"gram{i}", [P, Q, 2, P]) for i in range(2)]
        misc = psum("misc", [P, H1])
        misc_turn = misc[:, :].rearrange("p (k b) -> p k b", b=P)

        gathered = [sem(f"gathered{s}") for s in range(SLOTS)]
        idx_in = [sem(f"idx_in{i}") for i in range(2)]
        w_in = [sem(f"w_in{s}") for s in range(STAGE)]
        w_high, w_low = sem("w_high"), sem("w_low")
        ident_in, consts_in, cleared = sem("ident_in"), sem("consts_in"), sem("cleared")
        dense_in, slots_freed = sem("dense_in"), sem("slots_freed")
        x_turned, x_high, x_low = sem("x_turned"), sem("x_high"), sem("x_low")
        gram_done, gram_read = sem("gram_done"), sem("gram_read")
        gram_half = sem("gram_half")
        d_turned, full_done, pack_done = sem("d_turned"), sem("full_done"), sem("pack_done")
        pair_turned, pair_high, pair_low = sem("pair_turned"), sem("pair_high"), sem("pair_low")
        acc_done, h1_done = sem("acc_done"), sem("h1_done")
        h1_turned, h1t_done = sem("h1_turned"), sem("h1t_done")
        fc2_done, h2_done, y_done = sem("fc2_done"), sem("h2_done"), sem("y_done")
        y_turned, y_copied, stored = sem("y_turned"), sem("y_copied"), sem("stored")

        CONSTS = 3 * 16

        def slot_of(par, f):
            n = par * NF + f
            return n % SLOTS, n // SLOTS

        USES = 2 * NF // SLOTS


        block = ctx.enter_context(nc.Block())

        @block.sync
        def _(sp):
            def load_ids(m, par, c):
                sp.dma_start(idx[par][:, :], ids[c]).then_inc(idx_in[par], 16)

            def load_dense(c):
                for j in range(Q):
                    sp.dma_start(packed[FP * j:FP * j + FP, NPAIR:NPAIR + DENSE],
                                 dense[c, j]).then_inc(dense_in, 16)

            load_ids(0, 0, 0)
            sp.dma_start(ident[:, :], t["ident"]).then_inc(ident_in, 16)
            load_ids(0, 1, 1)
            for k in range(NK):
                if k >= STAGE:
                    sp.wait_ge(w_low, k - STAGE + 1)
                if k < NF:
                    sp.dma_start(w_stage[:, k % STAGE], t["w1"][k * P:(k + 1) * P]).then_inc(w_in[k % STAGE], 16)
                else:
                    n = P if k < NK - 1 else KLAST
                    a = (k - NF) * P
                    sp.dma_start(w_stage[0:n, k % STAGE], t["w1_tail"][a:a + n]).then_inc(w_in[k % STAGE], 16)
            sp.dma_start(w2[:, :, :], t["W_top2"].rearrange("(k p) n -> p k n", p=P)).then_inc(consts_in, 16)
            sp.dma_start(b2[:, :], t["b_top2"].to_broadcast([P, H2])).then_inc(consts_in, 16)
            sp.dma_start(w3[:, :], t["W_top3"].to_broadcast([P, H2])).then_inc(consts_in, 16)
            sp.wait_ge(cleared, 1)
            load_dense(0)

            def chunk(m, par, last=False):
                c = 2 * m + par
                if not last:
                    sp.wait_ge(x_turned, (c + 1) * NF)
                    load_ids(m, par, c + 2)
                if not (last and par == 1):
                    sp.wait_ge(pair_turned, c + 1)
                    load_dense(c + 1)

            with sp.Fori(0, NC // 2 - 1) as m:
                for par in range(2):
                    chunk(m, par)
            for par in range(2):
                chunk(NC // 2 - 1, par, last=True)
            sp.wait_ge(y_copied, 1)
            sp.dma_start(out.rearrange("(c p) o -> c (p o)", p=P), yt[:, :]).then_inc(stored, 16)
            sp.wait_ge(stored, 16)

        @block.gpsimd
        def _(pool):
            def gathers(m, par, first=False):
                pool.wait_ge(idx_in[par], 16 * (m + 1))
                for f in range(NF):
                    slot, _ = slot_of(par, f)
                    n = par * NF + f - SLOTS
                    if n >= 0 or not first:
                        pool.wait_ge(x_turned, m * (2 * NF) + n + 1)
                    if not first:
                        pool.sem_inc(slots_freed, 1)
                    nc.gpsimd.indirect_dma_start(
                        rows[:, slot, :], None, t[f"tbl_{f}"],
                        bass.IndirectOffsetOnAxis(ap=idx[par][:, f:f + 1], axis=0),
                    ).then_inc(gathered[slot], 16)

            for par in range(2):
                gathers(0, par, first=True)
            with pool.Fori(1, NC // 2) as m:
                for par in range(2):
                    gathers(m, par)

        @block.tensor
        def _(pe):
            def turn(m, par, f):
                slot, use = slot_of(par, f)
                pe.wait_ge(gathered[slot], (m * USES + use + 1) * 16)
                if f % GROUP == 0 and not (isinstance(m, int) and m == 0 and par == 0 and f == 0):
                    pe.wait_ge(x_low, (m * 2 + par) * NG + f // GROUP)
                nc.tensor.transpose(xt[:, f % GROUP, :], rows[:, slot, :], ident[:, :]).then_inc(x_turned, 1)

            def turn_group(m, par, g):
                for f in features(g):
                    turn(m, par, f)

            def fc1(m, par, fs, first=False):
                for f in fs:
                    if f == 0 and not first:
                        pe.wait_ge(h1_done, m * 2 + par - 1)
                    if f % GROUP == 0:
                        pe.wait_ge(x_low, (m * 2 + par) * NG + f // GROUP + 1)
                    if first and par == 0:
                        pe.wait_ge(w_low, f + 1)
                    xh, xl = xs[par][:, 0, :, f], xs[par][:, 1, :, f]
                    nc.tensor.matmul(acc[par][:, :], xh, w1h[:, f, :], start=f == 0, stop=False)
                    nc.tensor.matmul(acc[par][:, :], xh, w1l[:, f, :], start=False, stop=False)
                    nc.tensor.matmul(acc[par][:, :], xl, w1h[:, f, :], start=False, stop=False)

            def grams(m, par, q):
                if isinstance(m, int) and m == 0 and par == 0 and q < 2:
                    pe.wait_ge(cleared, 1)
                else:
                    pe.wait_ge(gram_read, (m * 2 + par) * QUADS + q - 1)
                for i in range(Q):
                    s = (q * Q + i) * Q
                    mm = nc.tensor.matmul(gram[q % 2][:, i, :, :], xs[par][:, 0, s:s + Q, :],
                                          xs[par][:, :, s:s + Q, :], start=True, stop=True)
                mm.then_inc(gram_done, 1)

            def turn_pairs(m, par, c):
                pe.wait_ge(pack_done, c + 1)
                pe.wait_ge(dense_in, (c + 1) * (Q * 16))
                if not (isinstance(c, int) and c == 0):
                    pe.wait_ge(h2_done, c)
                for k in range(KT):
                    tr = nc.tensor.transpose(misc_turn[:, k, :], packed[:, k * P:(k + 1) * P], ident[:, :])
                tr.then_inc(pair_turned, 1)

            def fc1_pairs(m, par, c):
                pe.wait_ge(pair_high, c + 1)
                if isinstance(c, int) and c == 0:
                    pe.wait_ge(w_low, NK)
                size = [P] * (KT - 1) + [KLAST]
                for k, n in enumerate(size):
                    nc.tensor.matmul(acc[par][:, :], zh[0:n, k, :], w1h[0:n, NF + k, :], start=False, stop=False)
                    nc.tensor.matmul(acc[par][:, :], zh[0:n, k, :], w1l[0:n, NF + k, :], start=False, stop=False)
                pe.wait_ge(pair_low, c + 1)
                for k, n in enumerate(size):
                    mm = nc.tensor.matmul(acc[par][:, :], zl[0:n, k, :], w1h[0:n, NF + k, :],
                                          start=False, stop=k == KT - 1)
                mm.then_inc(acc_done, 1)

            def turn_h1(c):
                pe.wait_ge(h1_done, c + 1)
                for k in range(H1 // P):
                    tr = nc.tensor.transpose(misc_turn[:, k, :], h1[:, k * P:(k + 1) * P], ident[:, :])
                tr.then_inc(h1_turned, 1)

            def fc2(c):
                pe.wait_ge(h1t_done, c + 1)
                if isinstance(c, int) and c == 0:
                    pe.wait_ge(consts_in, CONSTS)
                for k in range(H1 // P):
                    mm = nc.tensor.matmul(misc[:, 0:H2], h1t[:, k, :], w2[:, k, :], start=k == 0, stop=k == H1 // P - 1)
                mm.then_inc(fc2_done, 1)

            def before(m, par):
                return (m, 0) if par else (m - 1, 1)

            def chunk(m, par, first=False, last=False):
                c = 2 * m + par
                pm, pp = before(m, par)
                for g in range(NG):
                    fs = features(g)
                    turn_group(*((m, par, g + 1) if g + 1 < NG else (m, 1, 0) if par == 0 else (m + 1, 0, 0)))
                    if g == 0 and not first:
                        turn_h1(c - 2)
                    if g < QUADS // 2:
                        grams(pm, pp, 2 * g)
                    if g == 6:
                        fc1_pairs(pm, pp, c - 1)
                    fc1(m, par, fs[:2], first)
                    if g < QUADS // 2:
                        grams(pm, pp, 2 * g + 1)
                    if g == 1 and not first:
                        fc2(c - 2)
                    if g == 5:
                        turn_pairs(pm, pp, c - 1)
                    fc1(m, par, fs[2:], first)

            def first_chunk():
                turn_group(0, 0, 0)
                for g in range(NG):
                    fs, ahead = list(features(g)), list(features(g + 1)) if g + 1 < NG else []
                    for f in ahead[:2]:
                        turn(0, 0, f)
                    fc1(0, 0, fs[:1], first=True)
                    for f in ahead[2:]:
                        turn(0, 0, f)
                    fc1(0, 0, fs[1:], first=True)
                turn_group(0, 1, 0)

            def last_chunk():
                m, c = NC // 2 - 1, NC - 1
                turn_group(m, 1, 1)
                turn_h1(c - 2)
                for q in range(QUADS):
                    grams(m, 0, q)
                    fc1(m, 1, [q])
                    if q in (1, 3, 5):
                        turn_group(m, 1, (q + 3) // 2)
                    if q == 4:
                        fc2(c - 2)
                fc1(m, 1, [8])
                turn_group(m, 1, 5)
                fc1(m, 1, [9, 10])
                turn_group(m, 1, 6)
                fc1(m, 1, [11, 12, 13])
                turn_pairs(m, 0, c - 1)
                fc1(m, 1, [14, 15])
                fc1_pairs(m, 0, c - 1)
                grams(m, 1, 0)
                fc1(m, 1, [16])
                grams(m, 1, 1)
                turn_h1(c - 1)
                grams(m, 1, 2)
                fc1(m, 1, [17])
                grams(m, 1, 3)
                fc1(m, 1, [18])
                grams(m, 1, 4)
                fc2(c - 1)
                grams(m, 1, 5)
                fc1(m, 1, [19])
                grams(m, 1, 6)
                fc1(m, 1, [20])
                grams(m, 1, 7)
                fc1(m, 1, range(21, NF))
                turn_pairs(m, 1, c)
                fc1_pairs(m, 1, c)
                turn_h1(c)
                fc2(c)

            pe.wait_ge(ident_in, 16)
            first_chunk()
            chunk(0, 1, first=True)
            with pe.Fori(1, NC // 2 - 1) as m:
                for par in range(2):
                    chunk(m, par)
            chunk(NC // 2 - 1, 0)
            last_chunk()
            pe.wait_ge(y_done, NC)
            nc.tensor.transpose(misc[0:NC, 0:P], y[:, :], ident[:, :]).then_inc(y_turned, 1)

        @block.scalar
        def _(act):
            def high(m, par, g):
                n = len(features(g))
                a = g * GROUP
                act.wait_ge(x_turned, (m * 2 + par) * NF + a + n)
                nc.scalar.copy(xs[par][:, 0, :, a:a + n].rearrange("p s f -> p f s"), xt[:, 0:n, :]).then_inc(x_high, 1)

            def w_split(k):
                n = P if k < NK - 1 else KLAST
                act.wait_ge(w_in[k % STAGE], 16 * (k // STAGE + 1))
                nc.scalar.copy(w1h[0:n, k, :], w_stage[0:n, k % STAGE, :]).then_inc(w_high, 1)

            def half_high(c, q):
                act.wait_ge(gram_done, c * QUADS + q + 1)
                if q == 0:
                    if isinstance(c, int) and c == 0:
                        act.wait_ge(w_low, NK)
                    else:
                        act.wait_ge(pack_done, c)
                for j in range(Q):
                    a = FP * j
                    d = d_feat[a:a + FP, :, q * Q:(q + 1) * Q].rearrange("p g t -> p t g")
                    ins = nc.scalar.mul(d, gram[q % 2][a:a + FP, :, 0, a:a + NF], 0.5)
                ins.then_inc(gram_half, 1)

            def pack(c):
                act.wait_ge(full_done, 2 * (c + 1))
                if not (isinstance(c, int) and c == 0):
                    act.wait_ge(pair_turned, c)
                diagonals = bass.AP(full.tensor, full.offset + NF, [list(full.ap[0]), [NF, SHIFTS], [NF + 1, NF]])
                nc.scalar.copy(packed[:, 0:NPAIR].rearrange("p (k f) -> p k f", f=NF), diagonals).then_inc(pack_done, 1)

            def pairs_high(c):
                act.wait_ge(pair_turned, c + 1)
                nc.scalar.copy(zh[:, :, :].rearrange("p k (t j) -> p k j t", j=Q),
                               misc_turn[:, 0:KT, :].rearrange("p k (j t) -> p k j t", j=Q)).then_inc(pair_high, 1)

            def relu1(par, c):
                act.wait_ge(acc_done, c + 1)
                nc.scalar.activation(h1, acc[par][:, :], ACT.Relu).then_inc(h1_done, 1)

            def h1_copy(c):
                act.wait_ge(h1_turned, c + 1)
                nc.scalar.copy(h1t, misc_turn[:, :, :]).then_inc(h1t_done, 1)

            def chunk(m, par, first=False):
                c = 2 * m + par
                for g in range(NG):
                    high(*((m, par, g + 1) if g + 1 < NG else (m, 1, 0) if par == 0 else (m + 1, 0, 0)))
                    if g == 0 and not first:
                        h1_copy(c - 2)
                    if g < QUADS // 2:
                        half_high(c - 1, 2 * g)
                        half_high(c - 1, 2 * g + 1)
                    if g == 4:
                        pack(c - 1)
                    if g == 5:
                        pairs_high(c - 1)
                    if g == 6:
                        relu1(1 - par, c - 1)

            def first_chunk():
                k = 0
                for g in range(NG):
                    for k in range(k, min(g * GROUP + AHEAD, NK)):
                        w_split(k)
                    k = min(g * GROUP + AHEAD, NK)
                    high(0, 0, g)
                high(0, 1, 0)

            def last_chunk():
                m, c = NC // 2 - 1, NC - 1
                high(m, 1, 1)
                h1_copy(c - 2)
                for q in range(QUADS):
                    half_high(c - 1, q)
                    if q in (1, 3, 5):
                        high(m, 1, (q + 3) // 2)
                high(m, 1, 5)
                pack(c - 1)
                high(m, 1, 6)
                pairs_high(c - 1)
                relu1(0, c - 1)
                half_high(c, 0)
                half_high(c, 1)
                h1_copy(c - 1)
                for q in range(2, QUADS):
                    half_high(c, q)
                pack(c)
                pairs_high(c)
                relu1(1, c)
                h1_copy(c)

            first_chunk()
            chunk(0, 1, first=True)
            with act.Fori(1, NC // 2 - 1) as m:
                for par in range(2):
                    chunk(m, par)
            chunk(NC // 2 - 1, 0)
            last_chunk()

        @block.vector
        def _(dve):
            def low(m, par, g):
                n = len(features(g))
                a = g * GROUP
                dve.wait_ge(x_high, (m * 2 + par) * NG + g + 1)
                nc.vector.tensor_tensor(xs[par][:, 1, :, a:a + n].rearrange("p s f -> p f s"), xt[:, 0:n, :],
                                        xs[par][:, 0, :, a:a + n].rearrange("p s f -> p f s").bitcast(F32),
                                        ALU.subtract).then_inc(x_low, 1)

            def w_split(k):
                n = P if k < NK - 1 else KLAST
                dve.wait_ge(w_high, k + 1)
                nc.vector.tensor_tensor(w1l[0:n, k, :], w_stage[0:n, k % STAGE, :], w1h[0:n, k, :].bitcast(F32),
                                        ALU.subtract).then_inc(w_low, 1)

            def add_low(c, q):
                dve.wait_ge(gram_half, c * QUADS + q + 1)
                for j in range(Q):
                    a = FP * j
                    d = d_feat[a:a + FP, :, q * Q:(q + 1) * Q].rearrange("p g t -> p t g")
                    ins = nc.vector.tensor_tensor(d, gram[q % 2][a:a + FP, :, 1, a:a + NF], d, ALU.add)
                ins.then_inc(gram_read, 1)

            def fill_full(c):
                dve.wait_ge(gram_read, (c + 1) * QUADS)
                if not (isinstance(c, int) and c == 0):
                    dve.wait_ge(h2_done, c)
                    dve.wait_ge(y_done, c)
                nc.vector.transpose(d_samp.rearrange("p g f -> p (g f)"), d_feat.rearrange("p g t -> p (g t)")).then_inc(d_turned, 1)
                dve.wait_ge(d_turned, c + 1)
                for a, n in ((0, NF), (NF, SHIFTS)):
                    nc.vector.tensor_tensor(full[:, a:a + n, :], d_samp[:, 0:n, 0:NF],
                                            d_samp[:, 0:NF, 0:n].rearrange("p f g -> p g f"),
                                            ALU.add).then_inc(full_done, 1)

            def pairs_low(c):
                dve.wait_ge(pair_high, c + 1)
                nc.vector.tensor_tensor(zl[:, :, :].rearrange("p k (t j) -> p k j t", j=Q),
                                        misc_turn[:, 0:KT, :].rearrange("p k (j t) -> p k j t", j=Q),
                                        zh[:, :, :].rearrange("p k (t j) -> p k j t", j=Q).bitcast(F32),
                                        ALU.subtract).then_inc(pair_low, 1)

            def result(c):
                dve.wait_ge(fc2_done, c + 1)
                if isinstance(c, int) and c == 0:
                    dve.wait_ge(consts_in, CONSTS)
                nc.vector.tensor_tensor(h2, misc[:, 0:H2], b2[:, :], ALU.add).then_inc(h2_done, 1)
                dve.wait_ge(h2_done, c + 1)
                col = y[:, c:c + 1] if isinstance(c, int) else y[:, bass.ds(c, 1)]
                nc.vector.scalar_tensor_tensor(h2, h2, 0.0, w3[:, :], ALU.max, ALU.mult, accum_out=col).then_inc(y_done, 1)

            def chunk(m, par, first=False):
                c = 2 * m + par
                for g in range(NG):
                    low(*((m, par, g + 1) if g + 1 < NG else (m, 1, 0) if par == 0 else (m + 1, 0, 0)))
                    if g < QUADS // 2:
                        add_low(c - 1, 2 * g)
                        add_low(c - 1, 2 * g + 1)
                    if g == 1 and not first:
                        result(c - 2)
                    if g == 4:
                        fill_full(c - 1)
                    if g == 5:
                        pairs_low(c - 1)

            def first_chunk():
                k = 0
                for g in range(NG):
                    for k in range(k, min(g * GROUP + AHEAD, NK)):
                        w_split(k)
                    k = min(g * GROUP + AHEAD, NK)
                    low(0, 0, g)
                low(0, 1, 0)

            def last_chunk():
                m, c = NC // 2 - 1, NC - 1
                low(m, 1, 1)
                for q in range(QUADS):
                    add_low(c - 1, q)
                    if q in (1, 3, 5):
                        low(m, 1, (q + 3) // 2)
                    if q == 4:
                        result(c - 2)
                low(m, 1, 5)
                fill_full(c - 1)
                low(m, 1, 6)
                pairs_low(c - 1)
                for q in range(QUADS):
                    add_low(c, q)
                    if q == 4:
                        result(c - 1)
                fill_full(c)
                pairs_low(c)
                result(c)

            for x in xs:
                for part in range(2):
                    nc.vector.memset(x[:, part, :, NF:FP].bitcast(F32), 0.0)
            nc.vector.memset(packed[:, NPAIR + DENSE:TAIL], 1.0)
            nc.vector.memset(packed[:, TAIL:], 0.0).then_inc(cleared, 1)
            first_chunk()
            chunk(0, 1, first=True)
            with dve.Fori(1, NC // 2 - 1) as m:
                for par in range(2):
                    chunk(m, par)
            chunk(NC // 2 - 1, 0)
            last_chunk()
            dve.wait_ge(y_turned, 1)
            nc.vector.tensor_copy(yt[:, :], misc[0:NC, 0:P]).then_inc(y_copied, 1)


def kernel(**inputs):
    import numpy as _np
    import concourse.bacc as _bacc
    from concourse import mybir as _mybir
    from concourse.bass_utils import run_bass_kernel_spmd as _run

    nc = _bacc.Bacc("TRN2", target_bir_lowering=False, num_devices=1, dynamic_dma_scratch_size=8192)
    given = {k: _np.ascontiguousarray(v) for k, v in inputs.items()}
    w1 = given.pop("W_top1")
    b1 = given.pop("b_top1")
    at = {}
    for i, j in zip(*_np.triu_indices(NF, k=1)):
        at[int(i), int(j)] = len(at)
    order = [at[min(f, (f + k) % NF), max(f, (f + k) % NF)] for k in range(1, SHIFTS + 1) for f in range(NF)]
    pair_rows = w1[NF * P:NF * P + NPAIR][_np.array(order)]
    given["w1"] = w1[:NF * P]
    given["w1_tail"] = _np.concatenate([pair_rows, w1[NF * P + NPAIR:], b1[None, :]], axis=0)
    given["b_top2"] = given["b_top2"].reshape(1, H2)
    given["W_top3"] = given["W_top3"].reshape(1, H2)
    given["ident"] = _np.eye(P, dtype=_np.float32)
    arrays, tensors = {}, {}
    for name, a in given.items():
        a = _np.ascontiguousarray(a)
        arrays[f"in_{name}_dram"] = a
        tensors[name] = nc.dram_tensor(f"in_{name}_dram", a.shape, _mybir.dt.from_np(a.dtype), kind="ExternalInput").ap()
    out = nc.dram_tensor("out_0_dram", (BATCH, 1), F32, kind="ExternalOutput").ap()
    mlp_tower(nc, tensors, out)
    r = _run(nc, [arrays], core_ids=[0])
    return r.results[0]["out_0_dram"]
```

```python
from contextlib import ExitStack

import numpy as np

import concourse.bass as bass
from concourse import mybir

F32 = mybir.dt.float32
F32R = mybir.dt.float32r
ALU = mybir.AluOpType
ACT = mybir.ActivationFunctionType

P = 128
NF = 27
BATCH, DENSE, H1, H2 = 2048, 16, 512, 256
NC = BATCH // P
NPAIR = NF * (NF - 1) // 2
SHIFTS = NPAIR // NF
TAIL = NPAIR + DENSE + 1
KT = -(-TAIL // P)
KLAST = TAIL - (KT - 1) * P
NK = NF + KT
NT = NK + H2 * (H1 // P) // H1
GROUP = 4
NG = -(-NF // GROUP)
FP = 32
Q = P // FP
QUADS = P // (Q * Q)
SLOTS = 18
AHEAD = 6
LAST_GROUPS = {1: 1, 3: 2, 6: 3}
STAGE = 4


def features(g):
    return range(g * GROUP, min((g + 1) * GROUP, NF))


def mlp_tower(nc, t, out):
    ids = t["ids"].rearrange("(c p) f -> c p f", p=P)
    dense = t["dense_ctx"].rearrange("(c t j) d -> c j t d", t=FP, j=Q)

    with ExitStack() as ctx:
        def sb(name, shape, dt=F32):
            return ctx.enter_context(nc.sbuf_tensor(name, shape, dt))

        def psum(name, shape):
            return ctx.enter_context(nc.psum_tensor(name, shape, F32))

        def sem(name):
            return ctx.enter_context(nc.semaphore(name))

        w1h = sb("w1_high", [P, NK, H1], F32R)
        w1l = sb("w1_low", [P, NK, H1], F32R)
        xs = [sb(f"x_split{i}", [P, 2, P, FP], F32R) for i in range(2)]
        rows = sb("rows", [P, SLOTS, P])
        AW = (NF + SHIFTS) * NF
        arena = sb("arena", [P, max(AW + NF * FP, STAGE * H1)])
        w_stage = arena[:, 0:STAGE * H1].rearrange("p (s n) -> p s n", s=STAGE)
        d_feat = arena[:, 0:NF * FP].rearrange("p (g t) -> p g t", t=FP)
        full = arena[:, 0:AW].rearrange("p (g f) -> p g f", f=NF)
        d_samp = arena[:, AW:AW + NF * FP].rearrange("p (g f) -> p g f", f=FP)
        h1 = arena[:, AW:AW + H1]
        h2 = arena[:, AW:AW + H2]
        packed = sb("packed", [P, KT * P])
        th = sb("turned_high", [P, H1 // P, P], F32R)
        tl = sb("turned_low", [P, H1 // P, P], F32R)
        w2h = sb("w2_high", [P, H1 // P, H2], F32R)
        w2l = sb("w2_low", [P, H1 // P, H2], F32R)
        b2 = sb("b2", [P, H2])
        w3 = sb("w3", [P, H2])
        ident = sb("ident", [P, P])
        idx = [sb(f"idx{i}", [P, NF], t["ids"].dtype) for i in range(2)]
        y = sb("y", [P, NC])
        yt = arena[0:NC, AW:AW + P]

        acc = [psum(f"acc{i}", [P, H1]) for i in range(2)]
        xt = psum("x_turned_bank", [P, GROUP, P])
        gram = [psum(f"gram{i}", [P, Q, 2, P]) for i in range(2)]
        misc = psum("misc", [P, H1])
        misc_turn = misc[:, :].rearrange("p (k b) -> p k b", b=P)

        gathered = [sem(f"gathered{s}") for s in range(SLOTS)]
        idx_in = [sem(f"idx_in{i}") for i in range(2)]
        w_in = [sem(f"w_in{s}") for s in range(STAGE)]
        w_high, w_low = sem("w_high"), sem("w_low")
        ident_in, consts_in, cleared = sem("ident_in"), sem("consts_in"), sem("cleared")
        dense_in, slots_freed = sem("dense_in"), sem("slots_freed")
        x_turned, x_high, x_low = sem("x_turned"), sem("x_high"), sem("x_low")
        gram_done, gram_read = sem("gram_done"), sem("gram_read")
        gram_half = sem("gram_half")
        d_turned, full_done, pack_done = sem("d_turned"), sem("full_done"), sem("pack_done")
        pair_turned, pair_high, pair_low = sem("pair_turned"), sem("pair_high"), sem("pair_low")
        acc_done, h1_done = sem("acc_done"), sem("h1_done")
        h1_turned, h1t_high, h1t_low = sem("h1_turned"), sem("h1t_high"), sem("h1t_low")
        fc2_done, h2_done, y_done = sem("fc2_done"), sem("h2_done"), sem("y_done")
        y_turned, y_copied, stored = sem("y_turned"), sem("y_copied"), sem("stored")

        CONSTS = 2 * 16

        def tile_rows(k):
            return KLAST if k == NK - 1 else P

        def weights_before(g):
            return range((g - 1) * GROUP + AHEAD if g else 0, min(g * GROUP + AHEAD, NT))

        def split_tile(k):
            n = tile_rows(k)
            if k < NK:
                return w1h[0:n, k, :], w1l[0:n, k, :]
            ks = slice((k - NK) * (H1 // H2), (k - NK + 1) * (H1 // H2))
            return [w[:, ks, :].rearrange("p k n -> p (k n)") for w in (w2h, w2l)]

        def slot_of(par, f):
            n = par * NF + f
            return n % SLOTS, n // SLOTS

        USES = 2 * NF // SLOTS

        block = ctx.enter_context(nc.Block())

        @block.sync
        def _(sp):
            def load_ids(par, c):
                sp.dma_start(idx[par][:, :], ids[c]).then_inc(idx_in[par], 16)

            def load_dense(c):
                for j in range(Q):
                    sp.dma_start(packed[FP * j:FP * j + FP, NPAIR:NPAIR + DENSE],
                                 dense[c, j]).then_inc(dense_in, 16)

            load_ids(0, 0)
            sp.dma_start(ident[:, :], t["ident"]).then_inc(ident_in, 16)
            load_ids(1, 1)
            w2_tiles = t["W_top2"].rearrange("(t k p) n -> t p k n", p=P, k=H1 // H2)
            for k in range(NT):
                n, stage, a = tile_rows(k), w_stage[:, k % STAGE], (k - NF) * P
                if k >= STAGE:
                    sp.wait_ge(w_low, k - STAGE + 1)
                if k < NF:
                    sp.dma_start(stage, t["w1"][k * P:(k + 1) * P]).then_inc(w_in[k % STAGE], 16)
                elif k < NK:
                    sp.dma_start(stage[0:n], t["w1_tail"][a:a + n]).then_inc(w_in[k % STAGE], 16)
                else:
                    sp.dma_start(stage.rearrange("p (k n) -> p k n", n=H2),
                                 w2_tiles[k - NK]).then_inc(w_in[k % STAGE], 16)
            sp.dma_start(b2[:, :], t["b_top2"].to_broadcast([P, H2])).then_inc(consts_in, 16)
            sp.dma_start(w3[:, :], t["W_top3"].to_broadcast([P, H2])).then_inc(consts_in, 16)
            sp.wait_ge(cleared, 1)
            load_dense(0)

            def chunk(m, par, last=False):
                c = 2 * m + par
                if not last:
                    sp.wait_ge(x_turned, (c + 1) * NF)
                    load_ids(par, c + 2)
                if not (last and par == 1):
                    sp.wait_ge(pair_turned, c + 1)
                    load_dense(c + 1)

            with sp.Fori(0, NC // 2 - 1) as m:
                for par in range(2):
                    chunk(m, par)
            for par in range(2):
                chunk(NC // 2 - 1, par, last=True)
            sp.wait_ge(y_copied, 1)
            sp.dma_start(out.rearrange("(c p) o -> c (p o)", p=P), yt).then_inc(stored, 16)
            sp.wait_ge(stored, 16)

        @block.gpsimd
        def _(pool):
            def gathers(m, par, first=False):
                pool.wait_ge(idx_in[par], 16 * (m + 1))
                for f in range(NF):
                    slot, _ = slot_of(par, f)
                    n = par * NF + f - SLOTS
                    if n >= 0 or not first:
                        pool.wait_ge(x_turned, m * (2 * NF) + n + 1)
                    if not first:
                        pool.sem_inc(slots_freed, 1)
                    nc.gpsimd.indirect_dma_start(
                        rows[:, slot, :], None, t[f"tbl_{f}"],
                        bass.IndirectOffsetOnAxis(ap=idx[par][:, f:f + 1], axis=0),
                    ).then_inc(gathered[slot], 16)

            for par in range(2):
                gathers(0, par, first=True)
            with pool.Fori(1, NC // 2) as m:
                for par in range(2):
                    gathers(m, par)

        @block.tensor
        def _(pe):
            def turn(m, par, f):
                slot, use = slot_of(par, f)
                pe.wait_ge(gathered[slot], (m * USES + use + 1) * 16)
                if f % GROUP == 0 and not (isinstance(m, int) and m == 0 and par == 0 and f == 0):
                    pe.wait_ge(x_low, (m * 2 + par) * NG + f // GROUP)
                nc.tensor.transpose(xt[:, f % GROUP, :], rows[:, slot, :], ident[:, :]).then_inc(x_turned, 1)

            def turn_group(m, par, g):
                for f in features(g):
                    turn(m, par, f)

            def fc1(m, par, fs, first=False):
                for f in fs:
                    if f == 0 and not first:
                        pe.wait_ge(h1_done, m * 2 + par - 1)
                    if f % GROUP == 0:
                        pe.wait_ge(x_low, (m * 2 + par) * NG + f // GROUP + 1)
                    if first and par == 0:
                        pe.wait_ge(w_low, f + 1)
                    xh, xl = xs[par][:, 0, :, f], xs[par][:, 1, :, f]
                    nc.tensor.matmul(acc[par][:, :], xh, w1h[:, f, :], start=f == 0, stop=False)
                    nc.tensor.matmul(acc[par][:, :], xh, w1l[:, f, :], start=False, stop=False)
                    nc.tensor.matmul(acc[par][:, :], xl, w1h[:, f, :], start=False, stop=False)

            def grams(m, par, q):
                if isinstance(m, int) and m == 0 and par == 0 and q < 2:
                    pe.wait_ge(cleared, 1)
                else:
                    pe.wait_ge(gram_read, (m * 2 + par) * QUADS + q - 1)
                for i in range(Q):
                    s = (q * Q + i) * Q
                    mm = nc.tensor.matmul(gram[q % 2][:, i, :, :], xs[par][:, 0, s:s + Q, :],
                                          xs[par][:, :, s:s + Q, :], start=True, stop=True)
                mm.then_inc(gram_done, 1)

            def turn_pairs(c):
                pe.wait_ge(pack_done, c + 1)
                pe.wait_ge(dense_in, (c + 1) * (Q * 16))
                if not (isinstance(c, int) and c == 0):
                    pe.wait_ge(h2_done, c)
                for k in range(KT):
                    tr = nc.tensor.transpose(misc_turn[:, k, :], packed[:, k * P:(k + 1) * P], ident[:, :])
                tr.then_inc(pair_turned, 1)

            def fc1_pairs(par, c):
                pe.wait_ge(pair_high, c + 1)
                if isinstance(c, int) and c == 0:
                    pe.wait_ge(w_low, NK)
                size = [P] * (KT - 1) + [KLAST]
                for k, n in enumerate(size):
                    nc.tensor.matmul(acc[par][:, :], th[0:n, k, :], w1h[0:n, NF + k, :], start=False, stop=False)
                    nc.tensor.matmul(acc[par][:, :], th[0:n, k, :], w1l[0:n, NF + k, :], start=False, stop=False)
                pe.wait_ge(pair_low, c + 1)
                for k, n in enumerate(size):
                    mm = nc.tensor.matmul(acc[par][:, :], tl[0:n, k, :], w1h[0:n, NF + k, :],
                                          start=False, stop=k == KT - 1)
                mm.then_inc(acc_done, 1)

            def turn_h1(c):
                pe.wait_ge(h1_done, c + 1)
                for k in range(H1 // P):
                    tr = nc.tensor.transpose(misc_turn[:, k, :], h1[:, k * P:(k + 1) * P], ident[:, :])
                tr.then_inc(h1_turned, 1)

            def fc2(c, bank=misc):
                pe.wait_ge(h1t_high, c + 1)
                if bank is misc:
                    pe.wait_ge(h1t_low, c + 1)
                if isinstance(c, int) and c == 0:
                    pe.wait_ge(w_low, NT)
                for k in range(H1 // P):
                    nc.tensor.matmul(bank[:, 0:H2], th[:, k, :], w2h[:, k, :], start=k == 0, stop=False)
                    nc.tensor.matmul(bank[:, 0:H2], th[:, k, :], w2l[:, k, :], start=False, stop=False)
                if bank is not misc:
                    pe.wait_ge(h1t_low, c + 1)
                for k in range(H1 // P):
                    mm = nc.tensor.matmul(bank[:, 0:H2], tl[:, k, :], w2h[:, k, :], start=False, stop=k == H1 // P - 1)
                mm.then_inc(fc2_done, 1)

            def before(m, par):
                return (m, 0) if par else (m - 1, 1)

            def chunk(m, par, first=False):
                c = 2 * m + par
                pm, pp = before(m, par)
                for g in range(NG):
                    fs = features(g)
                    if g == 0 and not first:
                        turn_h1(c - 2)
                    if g < QUADS // 2:
                        grams(pm, pp, 2 * g)
                    ahead = (m, par, g + 1) if g + 1 < NG else (m, 1, 0) if par == 0 else (m + 1, 0, 0)
                    part = len(fs) - 2
                    if g >= QUADS // 2:
                        turn_group(*ahead)
                    fc1(m, par, fs[:part], first)
                    if g == 6:
                        fc1_pairs(pp, c - 1)
                    if g < QUADS // 2:
                        turn_group(*ahead)
                    if g < QUADS // 2:
                        grams(pm, pp, 2 * g + 1)
                    if g == 1 and not first:
                        fc2(c - 2)
                    fc1(m, par, fs[part:], first)
                    if g == 5:
                        turn_pairs(c - 1)

            def first_chunk():
                turn_group(0, 0, 0)
                for g in range(NG):
                    fs, ahead = list(features(g)), list(features(g + 1)) if g + 1 < NG else []
                    for f in ahead[:2]:
                        turn(0, 0, f)
                    fc1(0, 0, fs[:1], first=True)
                    for f in ahead[2:]:
                        turn(0, 0, f)
                    fc1(0, 0, fs[1:], first=True)
                turn_group(0, 1, 0)

            def last_chunk():
                m, c = NC // 2 - 1, NC - 1
                turn_h1(c - 2)
                for q in range(QUADS):
                    grams(m, 0, q)
                    fc1(m, 1, [q])
                    if q in LAST_GROUPS:
                        turn_group(m, 1, LAST_GROUPS[q])
                    if q == 2:
                        fc2(c - 2)
                fc1(m, 1, [8, 9])
                turn_group(m, 1, 4)
                fc1(m, 1, [10, 11, 12])
                turn_pairs(c - 1)
                fc1(m, 1, [13])
                turn_group(m, 1, 5)
                fc1_pairs(0, c - 1)
                fc1(m, 1, [14])
                turn_h1(c - 1)
                turn_group(m, 1, 6)
                fc1(m, 1, [15, 16])
                pe.wait_ge(x_low, NC * NG)
                for q in range(QUADS):
                    grams(m, 1, q)
                    if q == 1:
                        fc2(c - 1)
                    elif q:
                        fc1(m, 1, [15 + q])
                fc1(m, 1, range(15 + QUADS, NF))
                turn_pairs(c)
                fc1_pairs(1, c)
                turn_h1(c)
                fc2(c, acc[0])

            pe.wait_ge(ident_in, 16)
            first_chunk()
            chunk(0, 1, first=True)
            with pe.Fori(1, NC // 2 - 1) as m:
                for par in range(2):
                    chunk(m, par)
            chunk(NC // 2 - 1, 0)
            last_chunk()
            pe.wait_ge(y_done, NC)
            nc.tensor.transpose(misc[0:NC, 0:P], y[:, :], ident[:, :]).then_inc(y_turned, 1)

        @block.scalar
        def _(act):
            def high(m, par, g):
                n = len(features(g))
                a = g * GROUP
                act.wait_ge(x_turned, (m * 2 + par) * NF + a + n)
                nc.scalar.copy(xs[par][:, 0, :, a:a + n].rearrange("p s f -> p f s"), xt[:, 0:n, :]).then_inc(x_high, 1)

            def w_split(k):
                act.wait_ge(w_in[k % STAGE], 16 * (k // STAGE + 1))
                nc.scalar.copy(split_tile(k)[0], w_stage[0:tile_rows(k), k % STAGE, :]).then_inc(w_high, 1)

            def half_high(c, q):
                act.wait_ge(gram_done, c * QUADS + q + 1)
                if q == 0:
                    if isinstance(c, int) and c == 0:
                        act.wait_ge(w_low, NT)
                    else:
                        act.wait_ge(pack_done, c)
                for j in range(Q):
                    a = FP * j
                    d = d_feat[a:a + FP, :, q * Q:(q + 1) * Q].rearrange("p g t -> p t g")
                    nc.scalar.mul(d, gram[q % 2][a:a + FP, :, 0, a:a + NF], 0.5).then_inc(gram_half, 1)

            def pack(c):
                act.wait_ge(full_done, 2 * (c + 1))
                if not (isinstance(c, int) and c == 0):
                    act.wait_ge(pair_turned, c)
                diagonals = bass.AP(full.tensor, full.offset + NF, [list(full.ap[0]), [NF, SHIFTS], [NF + 1, NF]])
                nc.scalar.copy(packed[:, 0:NPAIR].rearrange("p (k f) -> p k f", f=NF), diagonals).then_inc(pack_done, 1)

            def pairs_high(c):
                act.wait_ge(pair_turned, c + 1)
                nc.scalar.copy(th[:, 0:KT, :].rearrange("p k (t j) -> p k j t", j=Q),
                               misc_turn[:, 0:KT, :].rearrange("p k (j t) -> p k j t", j=Q)).then_inc(pair_high, 1)

            def relu1(par, c):
                act.wait_ge(acc_done, c + 1)
                nc.scalar.activation(h1, acc[par][:, :], ACT.Relu).then_inc(h1_done, 1)

            def h1_copy(c):
                act.wait_ge(h1_turned, c + 1)
                nc.scalar.copy(th[:, :, :], misc_turn).then_inc(h1t_high, 1)

            def chunk(m, par, first=False):
                c = 2 * m + par
                for g in range(NG):
                    if g == 0 and not first:
                        h1_copy(c - 2)
                    if g < QUADS // 2:
                        half_high(c - 1, 2 * g)
                    high(*((m, par, g + 1) if g + 1 < NG else (m, 1, 0) if par == 0 else (m + 1, 0, 0)))
                    if g < QUADS // 2:
                        half_high(c - 1, 2 * g + 1)
                    if g == 4:
                        pack(c - 1)
                    if g == 5:
                        pairs_high(c - 1)
                    if g == 6:
                        relu1(1 - par, c - 1)

            def first_chunk():
                for g in range(NG + 1):
                    for k in weights_before(g):
                        w_split(k)
                    high(*((0, 0, g) if g < NG else (0, 1, 0)))

            def last_chunk():
                m, c = NC // 2 - 1, NC - 1
                h1_copy(c - 2)
                for q in range(QUADS):
                    half_high(c - 1, q)
                    if q in LAST_GROUPS:
                        high(m, 1, LAST_GROUPS[q])
                pack(c - 1)
                high(m, 1, 4)
                pairs_high(c - 1)
                high(m, 1, 5)
                relu1(0, c - 1)
                h1_copy(c - 1)
                high(m, 1, 6)
                for q in range(QUADS):
                    half_high(c, q)
                pack(c)
                pairs_high(c)
                relu1(1, c)
                h1_copy(c)

            first_chunk()
            chunk(0, 1, first=True)
            with act.Fori(1, NC // 2 - 1) as m:
                for par in range(2):
                    chunk(m, par)
            chunk(NC // 2 - 1, 0)
            last_chunk()

        @block.vector
        def _(dve):
            def low(m, par, g):
                n = len(features(g))
                a = g * GROUP
                dve.wait_ge(x_high, (m * 2 + par) * NG + g + 1)
                nc.vector.tensor_tensor(xs[par][:, 1, :, a:a + n].rearrange("p s f -> p f s"), xt[:, 0:n, :],
                                        xs[par][:, 0, :, a:a + n].rearrange("p s f -> p f s").bitcast(F32),
                                        ALU.subtract).then_inc(x_low, 1)

            def w_split(k):
                n = tile_rows(k)
                dve.wait_ge(w_high, k + 1)
                whole, (high, low_part) = w_stage[0:n, k % STAGE, :], split_tile(k)
                nc.vector.tensor_tensor(low_part, whole, high.bitcast(F32), ALU.subtract).then_inc(w_low, 1)

            def add_low(c, q):
                for j in range(Q):
                    a = FP * j
                    dve.wait_ge(gram_half, c * (QUADS * Q) + q * Q + j + 1)
                    d = d_feat[a:a + FP, :, q * Q:(q + 1) * Q].rearrange("p g t -> p t g")
                    ins = nc.vector.tensor_tensor(d, gram[q % 2][a:a + FP, :, 1, a:a + NF], d, ALU.add)
                ins.then_inc(gram_read, 1)

            def fill_full(c):
                dve.wait_ge(gram_read, (c + 1) * QUADS)
                if not (isinstance(c, int) and c == 0):
                    dve.wait_ge(h2_done, c)
                    dve.wait_ge(y_done, c)
                nc.vector.transpose(d_samp.rearrange("p g f -> p (g f)"), d_feat.rearrange("p g t -> p (g t)")).then_inc(d_turned, 1)
                dve.wait_ge(d_turned, c + 1)
                for a, n in ((0, NF), (NF, SHIFTS)):
                    nc.vector.tensor_tensor(full[:, a:a + n, :], d_samp[:, 0:n, 0:NF],
                                            d_samp[:, 0:NF, 0:n].rearrange("p f g -> p g f"),
                                            ALU.add).then_inc(full_done, 1)

            def pairs_low(c):
                dve.wait_ge(pair_high, c + 1)
                nc.vector.tensor_tensor(tl[:, 0:KT, :].rearrange("p k (t j) -> p k j t", j=Q),
                                        misc_turn[:, 0:KT, :].rearrange("p k (j t) -> p k j t", j=Q),
                                        th[:, 0:KT, :].rearrange("p k (t j) -> p k j t", j=Q).bitcast(F32),
                                        ALU.subtract).then_inc(pair_low, 1)

            def h1_low(c):
                dve.wait_ge(h1t_high, c + 1)
                nc.vector.tensor_tensor(tl[:, :, :], misc_turn, th[:, :, :].bitcast(F32), ALU.subtract).then_inc(h1t_low, 1)

            def result(c, bank=misc):
                dve.wait_ge(fc2_done, c + 1)
                if isinstance(c, int) and c == 0:
                    dve.wait_ge(consts_in, CONSTS)
                nc.vector.tensor_tensor(h2, bank[:, 0:H2], b2[:, :], ALU.add).then_inc(h2_done, 1)
                dve.wait_ge(h2_done, c + 1)
                col = y[:, c:c + 1] if isinstance(c, int) else y[:, bass.ds(c, 1)]
                nc.vector.scalar_tensor_tensor(h2, h2, 0.0, w3[:, :], ALU.max, ALU.mult, accum_out=col).then_inc(y_done, 1)

            def chunk(m, par, first=False):
                c = 2 * m + par
                for g in range(NG):
                    if g == 0 and not first:
                        h1_low(c - 2)
                    if g < QUADS // 2:
                        add_low(c - 1, 2 * g)
                    low(*((m, par, g + 1) if g + 1 < NG else (m, 1, 0) if par == 0 else (m + 1, 0, 0)))
                    if g < QUADS // 2:
                        add_low(c - 1, 2 * g + 1)
                    if g == 1 and not first:
                        result(c - 2)
                    if g == 4:
                        fill_full(c - 1)
                    if g == 5:
                        pairs_low(c - 1)

            def first_chunk():
                for g in range(NG + 1):
                    for k in weights_before(g):
                        w_split(k)
                    low(*((0, 0, g) if g < NG else (0, 1, 0)))

            def last_chunk():
                m, c = NC // 2 - 1, NC - 1
                h1_low(c - 2)
                for q in range(QUADS):
                    add_low(c - 1, q)
                    if q in LAST_GROUPS:
                        low(m, 1, LAST_GROUPS[q])
                    if q == 2:
                        result(c - 2)
                fill_full(c - 1)
                low(m, 1, 4)
                pairs_low(c - 1)
                low(m, 1, 5)
                h1_low(c - 1)
                low(m, 1, 6)
                for q in range(QUADS):
                    add_low(c, q)
                    if q == 1:
                        result(c - 1)
                fill_full(c)
                pairs_low(c)
                h1_low(c)
                result(c, acc[0])

            for x in xs:
                for part in range(2):
                    nc.vector.memset(x[:, part, :, NF:FP].bitcast(F32), 0.0)
            nc.vector.memset(packed[:, NPAIR + DENSE:TAIL], 1.0)
            nc.vector.memset(packed[:, TAIL:], 0.0).then_inc(cleared, 1)
            first_chunk()
            chunk(0, 1, first=True)
            with dve.Fori(1, NC // 2 - 1) as m:
                for par in range(2):
                    chunk(m, par)
            chunk(NC // 2 - 1, 0)
            last_chunk()
            dve.wait_ge(y_turned, 1)
            nc.vector.tensor_copy(yt, misc[0:NC, 0:P]).then_inc(y_copied, 1)


def kernel(**inputs):
    import numpy as _np
    import concourse.bacc as _bacc
    from concourse import mybir as _mybir
    from concourse.bass_utils import run_bass_kernel_spmd as _run

    nc = _bacc.Bacc("TRN2", target_bir_lowering=False, num_devices=1, dynamic_dma_scratch_size=6144)
    given = {k: _np.ascontiguousarray(v) for k, v in inputs.items()}
    w1 = given.pop("W_top1")
    b1 = given.pop("b_top1")
    at = {}
    for i, j in zip(*_np.triu_indices(NF, k=1)):
        at[int(i), int(j)] = len(at)
    order = [at[min(f, (f + k) % NF), max(f, (f + k) % NF)] for k in range(1, SHIFTS + 1) for f in range(NF)]
    pair_rows = w1[NF * P:NF * P + NPAIR][_np.array(order)]
    given["w1"] = w1[:NF * P]
    given["w1_tail"] = _np.concatenate([pair_rows, w1[NF * P + NPAIR:], b1[None, :]], axis=0)
    given["b_top2"] = given["b_top2"].reshape(1, H2)
    given["W_top3"] = given["W_top3"].reshape(1, H2)
    given["ident"] = _np.eye(P, dtype=_np.float32)
    arrays, tensors = {}, {}
    for name, a in given.items():
        a = _np.ascontiguousarray(a)
        arrays[f"in_{name}_dram"] = a
        tensors[name] = nc.dram_tensor(f"in_{name}_dram", a.shape, _mybir.dt.from_np(a.dtype), kind="ExternalInput").ap()
    out = nc.dram_tensor("out_0_dram", (BATCH, 1), F32, kind="ExternalOutput").ap()
    mlp_tower(nc, tensors, out)
    r = _run(nc, [arrays], core_ids=[0])
    return r.results[0]["out_0_dram"]
```
